# Optimizing a Trainium2 kernel written in Bass

```python
import numpy as np
import jax
import jax.numpy as jnp

def _softmax(x, axis=-1):
    return jax.nn.softmax(x, axis=axis)

def _gelu(x):
    return jax.nn.gelu(x, approximate=True)

def _silu(x):
    return jax.nn.silu(x)

def _sigmoid(x):
    return jax.nn.sigmoid(x)

def _layernorm(x, axis=-1, eps=1e-05):
    m = jnp.mean(x, axis=axis, keepdims=True)
    v = jnp.var(x, axis=axis, keepdims=True)
    return (x - m) / jnp.sqrt(v + eps)

def _scatter_add(tgt, idx, src, axis=0):
    return tgt.at[idx].add(src)

def _segment_sum(src, seg, n):
    return jax.ops.segment_sum(src, seg, n)
kernel_name = 'mk_adj_resnorm_d2_adj_r2_e39ee8'

def setup_inputs(seed: int=0):
    np.random.seed(seed)
    _w = jnp.asarray

    def _rec_inputs():
        import jax
        import jax.numpy as jnp
        _gk = jax.random.key(seed)
        x = -0.000929 + 1 * jax.random.normal(jax.random.fold_in(_gk, 1), (4096, 128), jnp.float32)
        _a = jax.random.bernoulli(jax.random.fold_in(_gk, 2), 0.00195312, (4096, 4096))
        _a = jnp.logical_or(_a, jnp.swapaxes(_a, -1, -2))
        _a = jnp.logical_or(_a, jnp.eye(4096, dtype=bool))
        _af = _a.astype(jnp.float32)
        _af = _af * jax.random.uniform(jax.random.fold_in(_gk, 3), (4096, 4096), jnp.float32, 0.05, 5.41998)
        adj = _af
        return (x, adj)
    x, adj = _rec_inputs()

    def _L0_gnn_setup():
        import jax, jax.numpy as jnp
        import numpy as np
        IN_F, OUT_F = (128, 128)
        R, LEV, N = (2, 2, 4096)
        JD = (R - 1) * LEV + 1
        key = jax.random.key(seed)
        ks = jax.random.split(key, 7)
        x = jax.random.normal(ks[0], (N, IN_F), dtype=jnp.float32)
        d_list = jax.random.uniform(ks[1], (JD, N), dtype=jnp.float32)
        U = jax.random.normal(ks[2], (N, N), dtype=jnp.float32)
        Vt = jax.random.normal(ks[3], (N, N), dtype=jnp.float32)
        bound = float(np.sqrt(6.0 / (IN_F + OUT_F)))
        weight = jax.random.uniform(ks[4], (IN_F, OUT_F), dtype=jnp.float32, minval=-bound, maxval=bound)
        filt = jax.random.uniform(ks[5], (JD, N), dtype=jnp.float32, minval=0.9, maxval=1.1)
        bias = jnp.zeros((OUT_F,), dtype=jnp.float32)
        return {'x': x, 'd_list': d_list, 'U': U, 'Vt': Vt, 'weight': weight, 'filt': filt, 'bias': bias}
    _L0_gnn_all = _L0_gnn_setup()
    _L0_gnn_in = {k: v for k, v in _L0_gnn_all.items() if k in ('d_list', 'weight', 'filt', 'bias')}
    del _L0_gnn_all

    def _L1_gnn_setup():
        import jax, jax.numpy as jnp
        import numpy as np
        N = 8192
        IN_DIM = 128
        OUT_DIM = 128

        def _message(X, A, W):
            deg = jnp.sum(A, axis=1, keepdims=True)
            A_norm = A / jnp.where(deg > 0, deg, 1.0)
            return A_norm @ X @ W
        key = jax.random.key(seed)
        k1, k2, k3, k4 = jax.random.split(key, 4)
        X = jax.random.normal(k1, (N, IN_DIM), dtype=jnp.float32)
        A = jax.random.uniform(k2, (N, N), dtype=jnp.float32)
        W_in = jax.random.normal(k3, (IN_DIM, OUT_DIM), dtype=jnp.float32) / np.sqrt(IN_DIM)
        W_out = jax.random.normal(k4, (IN_DIM, OUT_DIM), dtype=jnp.float32) / np.sqrt(IN_DIM)
        return {'X': X, 'A': A, 'W_in': W_in, 'W_out': W_out}
    _L1_gnn_all = _L1_gnn_setup()
    _L1_gnn_in = {k: v for k, v in _L1_gnn_all.items() if k in ('W_in', 'W_out')}
    del _L1_gnn_all
    return {'x': x, 'adj': adj, 'L0_gnn_d_list': _L0_gnn_in['d_list'], 'L0_gnn_weight': _L0_gnn_in['weight'], 'L0_gnn_filt': _L0_gnn_in['filt'], 'L0_gnn_bias': _L0_gnn_in['bias'], 'L1_gnn_W_in': _L1_gnn_in['W_in'], 'L1_gnn_W_out': _L1_gnn_in['W_out']}

def reference(x, adj, L0_gnn_d_list, L0_gnn_weight, L0_gnn_filt, L0_gnn_bias, L1_gnn_W_in, L1_gnn_W_out):
    import jax
    import jax.numpy as jnp

    def _L0_gnn_ref(x, d_list, U, Vt, weight, filt, bias):
        import jax, jax.numpy as jnp
        import numpy as np
        IN_F, OUT_F = (128, 128)
        R, LEV, N = (2, 2, 4096)
        JD = (R - 1) * LEV + 1
        xw = x @ weight
        Vxw = Vt @ xw
        scale = jnp.sum(d_list * filt * d_list, axis=0)
        out = U @ (scale[:, None] * Vxw)
        return out + bias

    def _L1_gnn_ref(X, A, W_in, W_out):
        import jax, jax.numpy as jnp
        import numpy as np
        N = 8192
        IN_DIM = 128
        OUT_DIM = 128

        def _message(X, A, W):
            deg = jnp.sum(A, axis=1, keepdims=True)
            A_norm = A / jnp.where(deg > 0, deg, 1.0)
            return A_norm @ X @ W
        X_in = _message(X, A, W_in)
        X_out = _message(X, A.T, W_out)
        return X_in + X_out
    x = _layernorm(x + _L0_gnn_ref(x, L0_gnn_d_list, adj, adj, L0_gnn_weight, L0_gnn_filt, L0_gnn_bias), axis=-1)
    x = _layernorm(x + _L1_gnn_ref(x, adj, L1_gnn_W_in, L1_gnn_W_out), axis=-1)
    return x

_drawn_inputs = setup_inputs


def setup_inputs(seed=0):
    import zlib

    import numpy as np

    out = dict(_drawn_inputs(seed))
    spreads = {'L0_gnn_bias': (0.0, 0.1)}
    factors = {}
    for name, (base, spread) in spreads.items():
        noise = np.random.default_rng([zlib.crc32(name.encode()), seed]).standard_normal(out[name].shape)
        drawn = base * np.exp(spread * noise) if base else spread * noise
        out[name] = jnp.asarray(drawn.astype(out[name].dtype))
    for name, factor in factors.items():
        out[name] = (out[name] * factor).astype(out[name].dtype)
    return out
```

```python
from contextlib import ExitStack

import concourse.bass as bass
from concourse import mybir

F32 = mybir.dt.float32
F32R = mybir.dt.float32r
ALU = mybir.AluOpType
ACT = mybir.ActivationFunctionType
AX_X = mybir.AxisListType.X

P = 128
TPB = 4
BLK = P * TPB
RING = 4
SLABS = 2
TPS = TPB // SLABS
LAG = 2
EPS = 1e-5


def graph_kernel(nc, x_t, adj_b, adjT_b, coef_t, W0, bias, W_in, W_out, ident_d, out):
    NB = adj_b.shape[0]
    NT = NB * TPB
    KD = coef_t.shape[2]

    phase1 = [((I + 1 + k) % NB, I) for I in range(NB) for k in range(NB)]
    phase2 = [(J, I) for I in range(NB - 2, -1, -1) for J in range(NB - 1, I, -1)]
    phase3 = [(I, J) for J in range(NB) for I in range(NB - 1, -1, -1)]
    phase4 = [(J, I) for I in range(NB) for J in range(I + 1)]
    N1 = len(phase1)
    N2 = N1 + len(phase2)
    N3 = N2 + len(phase3)
    N4 = N3 + len(phase4)
    chunks = ([(adjT_b, c) for c in phase1 + phase2] + [(adj_b, c) for c in phase3]
              + [(adjT_b, c) for c in phase4])

    last1 = {NB * I + NB - 1: I for I in range(NB)}
    last2 = {N1 + k: I for k, (J, I) in enumerate(phase2) if J == I + 1}
    last3 = {N2 + NB * J + NB - 1: J for J in range(NB)}
    last4 = {N3 + k: I for k, (J, I) in enumerate(phase4) if J == I}
    sum_at = {n + 1: I for n, I in last2.items() if I < NB - 2}
    sum_at[N1 + 2] = NB - 2
    norm_at = {n + 2: I for n, I in last2.items()}
    norm_at[N1 + 3] = NB - 2
    norm_at[N1 + 2] = NB - 1
    turn_at = {n + 1: I for n, I in last2.items()}
    turn_at[N1] = NB - 1

    def first4(I):
        return N3 + I * (I + 1) // 2

    def released(n):
        if n < N1 - 1 and n % NB == NB - 1:
            return n + 3
        if n < N1 and n >= NB and n % NB in (0, 1):
            return n
        return n + 1

    with ExitStack() as ctx:
        def sb(name, shape, dt=F32):
            return ctx.enter_context(nc.sbuf_tensor(name, shape, dt))

        def pb(name):
            return ctx.enter_context(nc.psum_tensor(name, [P, 2, BLK], F32))

        def sem(name):
            return ctx.enter_context(nc.semaphore(name))

        raw = sb("raw", [P, RING, TPB, BLK])
        hi = sb("hi", [P, RING, TPB, BLK], F32R)
        lo = sb("lo", [P, RING, TPB, BLK], F32R)
        x_hi = sb("x_hi", [P, NT, P], F32R)
        x_lo = sb("x_lo", [P, NT, P], F32R)
        v_hi = sb("v_hi", [P, NT, P], F32R)
        v_lo = sb("v_lo", [P, NT, P], F32R)
        rows = sb("rows", [P, NT, P])
        part = sb("part", [P, NB, BLK])
        turned = sb("turned", [P, 2, BLK])
        vtmp = sb("vtmp", [P, TPB, P])
        w0 = sb("w0", [P, P])
        w_in = sb("w_in", [P, P])
        w_out = sb("w_out", [P, P])
        ident = sb("ident", [P, P])
        bias_b = sb("bias_b", [P, P])
        coef = sb("coef", [P, 2, KD, NT])
        ctmp = sb("ctmp", [P, KD, NT])
        scale = sb("scale", [P, NT])
        colsum_p = sb("colsum_p", [P, NT, NB])
        rowsum_p = sb("rowsum_p", [P, NT, NB])
        deg = sb("deg", [P, 2, NT])
        dtmp = sb("dtmp", [P, 3, NT])
        stats = sb("stats", [P, TPB, 6])
        mv = sb("mv", [P, TPB, 2])
        rstd = sb("rstd", [P, TPB])
        var = sb("var", [P, TPB])
        std = sb("std", [P, TPB])
        newt = sb("newt", [P, TPB])
        accA = pb("accA")
        accB = pb("accB")
        nat = pb("nat")

        s_x = [sem(f"x_loaded{b}") for b in range(NB)]
        s_small = sem("small_loaded")
        s_raw = [sem(f"raw_loaded{r}") for r in range(RING)]
        s_xhi = sem("x_hi_ready")
        s_xlo = sem("x_lo_ready")
        s_hi = sem("hi_ready")
        s_lo = sem("lo_ready")
        s_rel = sem("chunks_released")
        s_z1 = sem("z_done1")
        s_zt = sem("z_turned_ready")
        s_w = sem("w_product_done")
        s_v = sem("v_ready")
        s_o = sem("o_done")
        s_os = sem("o_taken")
        s_t = sem("transposed")
        s_r = sem("residual_added")
        s_x1 = sem("x1_ready")
        s_ys = sem("y_saved")
        s_h = sem("h_ready")
        s_y4s = sem("y_summed")
        s_read = sem("last_read")
        s_var = sem("variance_ready")
        s_std = sem("deviation_ready")
        s_dve = sem("dve_step")
        s_out = sem("out_ready")
        s_st = sem("out_stored")

        small = [(w0[:], W0), (w_in[:], W_in), (w_out[:], W_out), (ident[:], ident_d),
                 (bias_b[:], bias.rearrange("(a f) -> a f", a=1).broadcast_to([P, P])), (coef[:], coef_t)]
        block = ctx.enter_context(nc.Block())

        @block.sync
        def _(sp):
            for n, (src, (K, C)) in enumerate(chunks):
                if n < NB:
                    b = phase1[n][0]
                    sp.dma_start(rows[:, TPB * b:TPB * b + TPB, :],
                                 x_t[:, TPB * b:TPB * b + TPB, :]).then_inc(s_x[b], 16)
                if n >= RING:
                    sp.wait_ge(s_lo, SLABS * (n - RING + 1))
                sp.dma_start(raw[:, n % RING], src[K, C]).then_inc(s_raw[n % RING], 16)
                if n == 1:
                    for dst, s in small:
                        sp.dma_start(dst, s).then_inc(s_small, 16)

        @block.gpsimd
        def _(pool):
            for I in range(NB):
                pool.wait_ge(s_out, I + 1)
                pool.dma_start(out[BLK * I:BLK * I + BLK, :].rearrange("(t p) f -> p t f", p=P),
                               rows[:, TPB * I:TPB * I + TPB, :]).then_inc(s_st, 16)
            pool.wait_ge(s_st, 16 * NB)

        @block.scalar
        def _(act):
            def split(n):
                K, C = chunks[n][1]
                act.wait_ge(s_raw[n % RING], 16 * (n // RING + 1))
                if n >= RING:
                    act.wait_ge(s_rel, released(n - RING))
                sums = colsum_p if n < N1 else rowsum_p if N2 <= n < N3 else None
                for s in range(SLABS):
                    if sums is None:
                        at = (n % RING, slice(TPS * s, TPS * s + TPS))
                        last = nc.scalar.activation(hi[:, at[0], at[1]], raw[:, at[0], at[1]], ACT.Copy)
                    else:
                        for t in range(TPS * s, TPS * s + TPS):
                            row = TPB * K + t
                            last = nc.scalar.activation(hi[:, n % RING, t], raw[:, n % RING, t], ACT.Copy,
                                                        accum_out=sums[:, row, C:C + 1])
                    last.then_inc(s_hi, 1)

            def deviation(k):
                act.wait_ge(s_var, k + 1)
                nc.scalar.activation(std[:], var[:], ACT.Sqrt).then_inc(s_std, 1)

            for n in range(N4):
                if n < NB:
                    b = phase1[n][0]
                    act.wait_ge(s_x[b], 16)
                    nc.scalar.activation(x_hi[:, TPB * b:TPB * b + TPB], rows[:, TPB * b:TPB * b + TPB],
                                         ACT.Copy).then_inc(s_xhi, 1)
                split(n)
                if n - 2 in last1:
                    I = last1[n - 2]
                    act.wait_ge(s_z1, I + 1)
                    if I >= 2:
                        act.wait_ge(s_w, I - 1)
                    nc.scalar.activation(turned[:, I % 2], accA[:, I % 2], ACT.Copy).then_inc(s_zt, 1)
                if n - 1 in norm_at:
                    deviation(NB - 1 - norm_at[n - 1])
                if n - 3 in last2:
                    I = last2[n - 3]
                    act.wait_ge(s_rel, released(n - 3))
                    nc.scalar.activation(part[:, I], accA[:, I % 2], ACT.Copy).then_inc(s_ys, 1)
                if n - 4 in last4:
                    deviation(NB + last4[n - 4])
                if n - 2 in last3:
                    J = last3[n - 2]
                    act.wait_ge(s_rel, released(n - 2))
                    if J < 2:
                        act.wait_ge(s_t, NB)
                    else:
                        act.wait_ge(s_w, NB + J - 1)
                    nc.scalar.activation(turned[:, J % 2], accB[:, J % 2], ACT.Copy).then_inc(s_zt, 1)
            deviation(2 * NB - 1)

        @block.vector
        def _(dve):
            steps = [0]
            norms = [0]

            def then(ins):
                steps[0] += 1
                ins.then_inc(s_dve, 1)
                dve.wait_ge(s_dve, steps[0])

            def low(n):
                for s in range(SLABS):
                    dve.wait_ge(s_hi, SLABS * n + s + 1)
                    at = slice(TPS * s, TPS * s + TPS)
                    nc.vector.tensor_tensor(lo[:, n % RING, at], raw[:, n % RING, at], hi[:, n % RING, at],
                                            ALU.subtract).then_inc(s_lo, 1)

            def inverse(sums, k):
                then(nc.vector.tensor_reduce(dtmp[:, 0], sums[:], AX_X, ALU.add))
                then(nc.vector.tensor_scalar(dtmp[:, 1], dtmp[:, 0], 0.0, None, ALU.is_gt))
                then(nc.vector.tensor_tensor(dtmp[:, 2], dtmp[:, 0], dtmp[:, 1], ALU.mult))
                then(nc.vector.tensor_scalar(dtmp[:, 1], dtmp[:, 1], -1.0, 1.0, ALU.mult, ALU.add))
                then(nc.vector.tensor_tensor(dtmp[:, 0], dtmp[:, 1], dtmp[:, 2], ALU.add))
                then(nc.vector.reciprocal(deg[:, k], dtmp[:, 0]))

            def scales():
                dve.wait_ge(s_small, 16 * len(small))
                then(nc.vector.tensor_tensor(ctmp[:], coef[:, 0], coef[:, 1], ALU.mult))
                then(nc.vector.tensor_tensor(ctmp[:], ctmp[:], coef[:, 0], ALU.mult))
                then(nc.vector.tensor_tensor(scale[:], ctmp[:, 0], ctmp[:, 1], ALU.add))
                for k in range(2, KD):
                    then(nc.vector.tensor_tensor(scale[:], scale[:], ctmp[:, k], ALU.add))

            def v_block(I):
                dve.wait_ge(s_w, I + 1)
                for t in range(TPB):
                    last = nc.vector.tensor_scalar(vtmp[:, t], nat[:, I % 2, P * t:P * t + P],
                                                   scale[:, TPB * I + t:TPB * I + t + 1], None, ALU.mult)
                then(last)
                at = slice(TPB * I, TPB * I + TPB)
                then(nc.vector.tensor_copy(v_hi[:, at], vtmp[:]))
                nc.vector.tensor_tensor(v_lo[:, at], vtmp[:], v_hi[:, at], ALU.subtract).then_inc(s_v, 1)
                for t in range(TPB * I, TPB * I + TPB):
                    last = nc.vector.tensor_tensor(rows[:, t], rows[:, t], bias_b[:], ALU.add)
                then(last)

            def o_sum(I):
                if I == NB - 1:
                    dve.wait_ge(s_rel, released(N1 - 1))
                    nc.vector.tensor_copy(turned[:, I % 2], accB[:, I % 2]).then_inc(s_os, 1)
                    return
                dve.wait_ge(s_o, NB - 1 - I)
                dve.wait_ge(s_os, I + 1)
                if NB - I - 2 > 0:
                    dve.wait_ge(s_t, NB - I - 2)
                nc.vector.tensor_tensor(turned[:, I % 2], accB[:, I % 2], part[:, I], ALU.add).then_inc(s_os, 1)

            def norm(I):
                for t in range(TPB):
                    last = nc.vector.bn_stats(stats[:, t], rows[:, TPB * I + t])
                then(last)
                for t in range(TPB):
                    last = nc.vector.bn_aggr(mv[:, t], stats[:, t])
                then(last)
                norms[0] += 1
                nc.vector.tensor_scalar(var[:], mv[:, :, 1], EPS, None, ALU.add).then_inc(s_var, 1)
                dve.wait_ge(s_std, norms[0])
                then(nc.vector.reciprocal(rstd[:], std[:]))
                then(nc.vector.tensor_tensor(newt[:], var[:], rstd[:], ALU.mult))
                then(nc.vector.tensor_tensor(newt[:], newt[:], rstd[:], ALU.mult))
                then(nc.vector.tensor_scalar(newt[:], newt[:], -0.5, 1.5, ALU.mult, ALU.add))
                then(nc.vector.tensor_tensor(rstd[:], rstd[:], newt[:], ALU.mult))
                for t in range(TPB):
                    last = nc.vector.tensor_scalar(rows[:, TPB * I + t], rows[:, TPB * I + t], mv[:, t, 0:1],
                                                   rstd[:, t:t + 1], ALU.subtract, ALU.mult)
                return last

            def x1_block(I):
                at = slice(TPB * I, TPB * I + TPB)
                dve.wait_ge(s_t, NB - I)
                ins = nc.vector.tensor_tensor(rows[:, at], nat[:, I % 2].rearrange("p (t f) -> p t f", t=TPB),
                                              rows[:, at], ALU.add)
                ins.then_inc(s_r, 1)
                dve.wait_ge(s_r, NB - I)
                then(norm(I))
                then(nc.vector.tensor_copy(x_hi[:, at], rows[:, at]))
                nc.vector.tensor_tensor(x_lo[:, at], rows[:, at], x_hi[:, at], ALU.subtract).then_inc(s_x1, 1)

            def h_block(J):
                dve.wait_ge(s_w, NB + J + 1)
                for t in range(TPB):
                    r = TPB * J + t
                    last = nc.vector.scalar_tensor_tensor(rows[:, r], nat[:, J % 2, P * t:P * t + P],
                                                          deg[:, 0, r:r + 1], rows[:, r], ALU.mult, ALU.add)
                last.then_inc(s_h, 1)

            def y_total(I):
                dve.wait_ge(s_rel, released(first4(I + 1) - 1))
                dve.wait_ge(s_w, 2 * NB + I - 1)
                if I < NB - 1:
                    dve.wait_ge(s_ys, NB - 1)
                    ins = nc.vector.tensor_tensor(turned[:, I % 2], accA[:, I % 2], part[:, I], ALU.add)
                else:
                    ins = nc.vector.tensor_copy(turned[:, I % 2], accA[:, I % 2])
                ins.then_inc(s_y4s, 1)

            def out_block(I):
                dve.wait_ge(s_w, 2 * NB + I + 1)
                dve.wait_ge(s_h, NB)
                for t in range(TPB):
                    r = TPB * I + t
                    last = nc.vector.scalar_tensor_tensor(rows[:, r], nat[:, I % 2, P * t:P * t + P],
                                                          deg[:, 1, r:r + 1], rows[:, r], ALU.mult, ALU.add)
                last.then_inc(s_read, 1)
                dve.wait_ge(s_read, I + 1)
                norm(I).then_inc(s_out, 1)

            for n in range(N4):
                if n < NB:
                    b = phase1[n][0]
                    at = slice(TPB * b, TPB * b + TPB)
                    dve.wait_ge(s_xhi, n + 1)
                    nc.vector.tensor_tensor(x_lo[:, at], rows[:, at], x_hi[:, at],
                                            ALU.subtract).then_inc(s_xlo, 1)
                low(n)
                if n == 3:
                    scales()
                if n - 2 in last1:
                    v_block(last1[n - 2])
                if n - 3 in last1 and n - 3 < N1 - 1:
                    I = last1[n - 3]
                    dve.wait_ge(s_rel, released(n - 3))
                    nc.vector.tensor_copy(part[:, I], accB[:, I % 2]).then_inc(s_os, 1)
                if n == N1 + 1:
                    o_sum(NB - 1)
                if n in sum_at:
                    o_sum(sum_at[n])
                if n in norm_at:
                    x1_block(norm_at[n])
                if n == N1 + 5:
                    inverse(colsum_p, 0)
                if n == N3:
                    inverse(rowsum_p, 1)
                if n - 2 in last3:
                    h_block(last3[n - 2])
                if n - 2 in last4:
                    y_total(last4[n - 2])
                if n - 3 in last4:
                    out_block(last4[n - 3])
            y_total(NB - 1)
            out_block(NB - 1)

        @block.tensor
        def _(pe):
            def product(acc, r_hi, r_lo, K, n, first, last):
                for s in range(SLABS):
                    tiles = range(TPS * s, TPS * s + TPS)
                    pe.wait_ge(s_hi, SLABS * n + s + 1)
                    for t in tiles:
                        nc.tensor.matmul(acc, r_hi[:, TPB * K + t], hi[:, n % RING, t],
                                         start=(first and t == 0), stop=False)
                        nc.tensor.matmul(acc, r_lo[:, TPB * K + t], hi[:, n % RING, t], start=False, stop=False)
                    pe.wait_ge(s_lo, SLABS * n + s + 1)
                    for t in tiles:
                        mm = nc.tensor.matmul(acc, r_hi[:, TPB * K + t], lo[:, n % RING, t], start=False,
                                              stop=(last and t == TPB - 1))
                return mm

            def by_rows(b, w):
                for t in range(TPB):
                    mm = nc.tensor.matmul(nat[:, b, P * t:P * t + P], turned[:, b, P * t:P * t + P], w[:],
                                          start=True, stop=True)
                mm.then_inc(s_w, 1)

            def w0_block(I):
                pe.wait_ge(s_zt, I + 1)
                pe.wait_ge(s_small, 16 * len(small))
                if I >= 2:
                    pe.wait_ge(s_v, I - 1)
                by_rows(I % 2, w0)

            def diagonal(I):
                pe.wait_ge(s_v, I + 1)
                product(accB[:, I % 2], v_hi, v_lo, I, NB * I + NB - 1, I == 0, True).then_inc(s_rel, 1)

            def transposes(I):
                pe.wait_ge(s_os, 2 * NB - 1 - I)
                if NB - I - 2 > 0:
                    pe.wait_ge(s_r, NB - I - 2)
                for t in range(TPB):
                    mm = nc.tensor.transpose(nat[:, I % 2, P * t:P * t + P], turned[:, I % 2, P * t:P * t + P],
                                             ident[:])
                mm.then_inc(s_t, 1)

            def convolve2(n):
                J, I = chunks[n][1]
                pe.wait_ge(s_x1, NB - J)
                if J == NB - 1 and NB - 3 - I > 0:
                    pe.wait_ge(s_ys, NB - 3 - I)
                product(accA[:, I % 2], x_hi, x_lo, J, n, J == NB - 1, J == I + 1).then_inc(s_rel, 1)

            for n in range(N1):
                J, I = chunks[n][1]
                if n < NB:
                    pe.wait_ge(s_xlo, n + 1)
                if n % NB == 0 and I >= 2:
                    pe.wait_ge(s_zt, I - 1)
                mm = product(accA[:, I % 2], x_hi, x_lo, J, n, n % NB == 0, J == I)
                if J == I:
                    mm.then_inc(s_z1, 1)
                elif J > I:
                    mm.then_inc(s_rel, 1)
                else:
                    pe.wait_ge(s_v, J + 1)
                    if J == 0 and I >= 2:
                        pe.wait_ge(s_os, I - 1)
                    product(accB[:, I % 2], v_hi, v_lo, J, n, J == 0, False).then_inc(s_rel, 1)
                if n >= NB and n % NB == 0:
                    w0_block(I - 1)
                if n >= NB and n % NB == 1:
                    diagonal(I - 1)
            w0_block(NB - 1)
            diagonal(NB - 1)

            for n in range(N1, N2):
                J, I = chunks[n][1]
                if J == NB - 1:
                    pe.wait_ge(s_os, 2 * NB - 3 - I)
                mm = product(accB[:, I % 2], v_hi, v_lo, J, n, J == NB - 1, J == I + 1)
                if J == I + 1:
                    mm.then_inc(s_o, 1)
                if n in turn_at:
                    transposes(turn_at[n])
                if n >= N1 + LAG:
                    convolve2(n - LAG)
            convolve2(N2 - 2)
            transposes(0)
            convolve2(N2 - 1)

            def w_out_block(J):
                pe.wait_ge(s_zt, NB + J + 1)
                if J < 2:
                    pe.wait_ge(s_r, NB)
                else:
                    pe.wait_ge(s_h, J - 1)
                by_rows(J % 2, w_out)

            def w_in_block(I):
                pe.wait_ge(s_y4s, I + 1)
                if I < 2:
                    pe.wait_ge(s_h, NB)
                else:
                    pe.wait_ge(s_read, I - 1)
                by_rows(I % 2, w_in)

            for n in range(N2, N3):
                I, J = chunks[n][1]
                if J == 0:
                    pe.wait_ge(s_x1, NB - I)
                if I == NB - 1 and J >= 2:
                    pe.wait_ge(s_zt, NB + J - 1)
                product(accB[:, J % 2], x_hi, x_lo, I, n, I == NB - 1, I == 0).then_inc(s_rel, 1)
                if n - 2 in last3:
                    w_out_block(last3[n - 2])

            for n in range(N3, N4):
                J, I = chunks[n][1]
                if J == 0:
                    pe.wait_ge(s_ys, NB - 1)
                    if I >= 2:
                        pe.wait_ge(s_y4s, I - 1)
                product(accA[:, I % 2], x_hi, x_lo, J, n, J == 0, J == I).then_inc(s_rel, 1)
                if n - 2 in last3:
                    w_out_block(last3[n - 2])
                if n - 2 in last4:
                    w_in_block(last4[n - 2])
            w_in_block(NB - 1)


def kernel(x, adj, L0_gnn_d_list, L0_gnn_weight, L0_gnn_filt, L0_gnn_bias, L1_gnn_W_in, L1_gnn_W_out):
    import numpy as np
    import concourse.bacc as bacc
    from concourse import mybir
    from concourse.bass_utils import run_bass_kernel_spmd

    x, adj = np.asarray(x), np.asarray(adj)
    N, F = x.shape
    NB, NT = N // BLK, N // P
    levels = [np.asarray(a).reshape(-1, NT, P).transpose(2, 0, 1) for a in (L0_gnn_d_list, L0_gnn_filt)]
    arrays = {
        "x_t": x.reshape(NT, P, F).transpose(1, 0, 2),
        "adj_b": adj.reshape(NB, TPB, P, NB, BLK).transpose(0, 3, 2, 1, 4),
        "adjT_b": adj.reshape(NB, BLK, NB, TPB, P).transpose(2, 0, 4, 3, 1),
        "coef_t": np.stack(levels, axis=1),
        "W0": np.asarray(L0_gnn_weight),
        "bias": np.asarray(L0_gnn_bias),
        "W_in": np.asarray(L1_gnn_W_in),
        "W_out": np.asarray(L1_gnn_W_out),
        "ident": np.eye(P, dtype=np.float32),
    }
    nc = bacc.Bacc("TRN2", target_bir_lowering=False, num_devices=1)
    named, args = {}, []
    for name, a in arrays.items():
        named[f"in_{name}"] = np.ascontiguousarray(a)
        args.append(nc.dram_tensor(f"in_{name}", a.shape, mybir.dt.from_np(a.dtype), kind="ExternalInput").ap())
    args.append(nc.dram_tensor("out", (N, F), mybir.dt.float32, kind="ExternalOutput").ap())
    graph_kernel(nc, *args)
    return run_bass_kernel_spmd(nc, [named], core_ids=[0]).results[0]["out"]
```

```python
from contextlib import ExitStack

import concourse.bass as bass
from concourse import mybir

F32 = mybir.dt.float32
F32R = mybir.dt.float32r
ALU = mybir.AluOpType
ACT = mybir.ActivationFunctionType
AX_X = mybir.AxisListType.X

P = 128
TPB = 4
BLK = P * TPB
RING = 4
SLABS = 2
TPS = TPB // SLABS
HELD = 2
LAG = 2
STORE_LAG = 14
EPS = 1e-5


def graph_kernel(nc, x_t, adj_b, adjT_b, coef_t, W0, bias, W_in, W_out, ident_d, out):
    NB = adj_b.shape[0]
    NT = NB * TPB
    KD = coef_t.shape[2]

    phase1 = [((I + 1 + k) % NB, I) for I in range(NB) for k in range(NB)]
    phase2 = [(J, I) for I in range(NB - 2, -1, -1) for J in range(NB - 1, I, -1)]
    phase3 = [(I, J) for J in range(NB) for I in range(NB - 1, -1, -1)]
    phase4 = [(J, I) for I in range(NB) for J in range(I + 1)]
    N1 = len(phase1)
    N2 = N1 + len(phase2)
    N3 = N2 + len(phase3)
    N4 = N3 + len(phase4)
    chunks = phase1 + phase2 + phase3 + phase4
    assert NB % RING == 0 and N2 % RING == 0


    last1 = {NB * I + NB - 1: I for I in range(NB)}
    last2 = {N1 + k: I for k, (J, I) in enumerate(phase2) if J == I + 1}
    last4 = {N3 + k: I for k, (J, I) in enumerate(phase4) if J == I}
    sum_at = {n + 1: I for n, I in last2.items() if I < NB - 2}
    sum_at[N1 + 2] = NB - 2
    norm_at = {n + 2: I for n, I in last2.items()}
    norm_at[N1 + 3] = NB - 2
    norm_at[N1 + 2] = NB - 1
    parts_at = {n + (1 if I < NB - 3 else 0): I for n, I in norm_at.items()}
    z_at = {n + (2 if I < NB - 1 else 1): I for n, I in last1.items()}
    turn_at = {n + 1: I for n, I in last2.items()}
    turn_at[N1] = NB - 1

    def first4(I):
        return N3 + I * (I + 1) // 2

    def released(n):
        if n < N1 - 1 and n % NB == NB - 1:
            return n + 3
        if n < N1 and n >= NB and n % NB in (0, 1):
            return n
        return n + 1

    with ExitStack() as ctx:
        def sb(name, shape, dt=F32):
            return ctx.enter_context(nc.sbuf_tensor(name, shape, dt))

        def pb(name):
            return ctx.enter_context(nc.psum_tensor(name, [P, 2, BLK], F32))

        def sem(name):
            return ctx.enter_context(nc.semaphore(name))

        raw = sb("raw", [P, RING, TPB, BLK])
        hi = sb("hi", [P, RING, TPB, BLK], F32R)
        lo = sb("lo", [P, RING, TPB, BLK], F32R)
        x_hi = sb("x_hi", [P, NT, P], F32R)
        x_lo = sb("x_lo", [P, NT, P], F32R)
        v_hi = sb("v_hi", [P, NT, P], F32R)
        v_lo = sb("v_lo", [P, NT, P], F32R)
        rows = sb("rows", [P, NT, P])
        part = sb("part", [P, NB - 1, BLK])
        turned = sb("turned", [P, 2, BLK])
        w0 = sb("w0", [P, P])
        w_in = sb("w_in", [P, P])
        w_out = sb("w_out", [P, P])
        ident = sb("ident", [P, P])
        bias_b = sb("bias_b", [P, P])
        coef = sb("coef", [P, 2, KD, NT])
        ctmp = sb("ctmp", [P, KD, NT])
        scale = sb("scale", [P, NT])
        sums = sb("sums", [P, NT, NB])
        deg = sb("deg", [P, 2, NT])
        dtmp = sb("dtmp", [P, 3, NT])
        stats = sb("stats", [P, TPB, 6])
        mv = sb("mv", [P, TPB, 2])
        rstd = sb("rstd", [P, TPB])
        var = sb("var", [P, TPB])
        std = sb("std", [P, TPB])
        newt = sb("newt", [P, TPB])
        accA = pb("accA")
        accB = pb("accB")
        nat = pb("nat")

        s_x = [sem(f"x_loaded{b}") for b in range(NB)]
        s_small = sem("small_loaded")
        s_raw = [sem(f"raw_loaded{r}") for r in range(RING)]
        s_st = sem("out_stored")
        s_xhi = sem("x_hi_ready")
        s_hi = sem("hi_ready")
        s_zt = sem("z_turned_ready")
        s_ys = sem("y_saved")
        s_y4s = sem("y_turned_ready")
        s_std = sem("deviation_ready")
        s_xlo = sem("x_lo_ready")
        s_lo = sem("lo_ready")
        s_v = sem("v_ready")
        s_os = sem("o_taken")
        s_nat = sem("nat_read")
        s_x1 = sem("x1_ready")
        s_var = sem("variance_ready")
        s_out = sem("out_ready")
        s_dve = sem("dve_step")
        s_rel = sem("chunks_released")
        s_z1 = sem("z_done")
        s_o = sem("o_done")
        s_w = sem("w_product_done")
        s_t = sem("transposed")

        small = [(w0[:], W0), (w_in[:], W_in), (w_out[:], W_out), (ident[:], ident_d),
                 (bias_b[:], bias.rearrange("(a f) -> a f", a=1).broadcast_to([P, P])), (coef[:], coef_t)]
        block = ctx.enter_context(nc.Block())

        @block.sync
        def _(sp):
            def load(n, slot, src):
                if n >= RING:
                    sp.wait_ge(s_lo, SLABS * (n - RING + 1))
                sp.dma_start(raw[:, slot], src).then_inc(s_raw[slot], 16)

            def store(I):
                sp.wait_ge(s_out, I + 1)
                sp.dma_start(out[BLK * I:BLK * I + BLK, :].rearrange("(t p) f -> p t f", p=P),
                             rows[:, TPB * I:TPB * I + TPB, :]).then_inc(s_st, 16)

            for n in range(N2):
                if n < NB:
                    b = phase1[n][0]
                    sp.dma_start(rows[:, TPB * b:TPB * b + TPB, :],
                                 x_t[:, TPB * b:TPB * b + TPB, :]).then_inc(s_x[b], 16)
                load(n, n % RING, adjT_b[chunks[n][0], chunks[n][1]])
                if n == NB - 1:
                    for dst, s in small:
                        sp.dma_start(dst, s).then_inc(s_small, 16)
            for n in range(N2, N3):
                load(n, n % RING, adj_b[chunks[n][0], chunks[n][1]])
            for n in range(N3, N4):
                load(n, n % RING, adjT_b[chunks[n][0], chunks[n][1]])
                if n - STORE_LAG in last4:
                    store(last4[n - STORE_LAG])
            for I in range(NB):
                if first4(I + 1) - 1 + STORE_LAG >= N4:
                    store(I)
            sp.wait_ge(s_st, 16 * NB)

        @block.scalar
        def _(act):
            def split(slot, turn, free, K, C, summed):
                act.wait_ge(s_raw[slot], 16 * (turn + 1))
                if free is not None:
                    act.wait_ge(s_rel, free)
                for s in range(SLABS):
                    if not summed:
                        at = slice(TPS * s, TPS * s + TPS)
                        last = nc.scalar.activation(hi[:, slot, at], raw[:, slot, at], ACT.Copy)
                    else:
                        for t in range(TPS * s, TPS * s + TPS):
                            last = nc.scalar.activation(hi[:, slot, t], raw[:, slot, t], ACT.Copy,
                                                        accum_out=sums[:, TPB * K + t, bass.ds(C, 1)])
                    last.then_inc(s_hi, 1)

            def deviation(k):
                act.wait_ge(s_var, k + 1)
                nc.scalar.activation(std[:], var[:], ACT.Sqrt).then_inc(s_std, 1)

            def beside(n):
                if n in z_at:
                    I = z_at[n]
                    act.wait_ge(s_z1, I + 1)
                    if I >= 2:
                        act.wait_ge(s_w, I - 1)
                    nc.scalar.activation(turned[:, I % 2], accA[:, I % 2], ACT.Copy).then_inc(s_zt, 1)
                if n - 1 in norm_at:
                    deviation(NB - 1 - norm_at[n - 1])
                if n - 3 in last2:
                    I = last2[n - 3]
                    act.wait_ge(s_rel, released(n - 3))
                    nc.scalar.activation(part[:, I], accA[:, I % 2], ACT.Copy).then_inc(s_ys, 1)

            def save_z(J, b, n):
                act.wait_ge(s_rel, n - 1)
                if isinstance(J, int) and J < 2:
                    act.wait_ge(s_t, NB)
                else:
                    act.wait_ge(s_w, NB - 1 + J)
                nc.scalar.activation(turned[:, b], accB[:, b], ACT.Copy).then_inc(s_zt, 1)

            def save_y(I):
                act.wait_ge(s_rel, released(first4(I + 1) - 1))
                act.wait_ge(s_w, 2 * NB - 1 + I)
                nc.scalar.activation(turned[:, I % 2], accA[:, I % 2], ACT.Copy).then_inc(s_y4s, 1)

            def block3(J, b, first=False):
                for k in range(NB):
                    n = N2 + NB * J + k
                    split(k % RING, (N2 + k) // RING + NB // RING * J, n - RING + 1, NB - 1 - k, J, True)
                    if first:
                        beside(n)
                    elif k == 1:
                        save_z(J - 1, 1 - b, n)

            for n in range(N2):
                if n < NB:
                    b = phase1[n][0]
                    act.wait_ge(s_x[b], 16)
                    nc.scalar.activation(x_hi[:, TPB * b:TPB * b + TPB], rows[:, TPB * b:TPB * b + TPB],
                                         ACT.Copy).then_inc(s_xhi, 1)
                split(n % RING, n // RING, released(n - RING) if n >= RING else None, *chunks[n], n < N1)
                beside(n)
            block3(0, 0, first=True)
            block3(1, 1)
            with act.Fori(1, NB // 2) as pair:
                block3(2 * pair, 0)
                block3(2 * pair + 1, 1)
            for n in range(N3, N4):
                split(n % RING, n // RING, released(n - RING), *chunks[n], False)
                if n == N3 + 1:
                    save_z(NB - 1, 1, n)
                if n - 5 in last4:
                    deviation(NB + last4[n - 5])
                if n - 2 in last4:
                    save_y(last4[n - 2])
            save_y(NB - 1)
            deviation(2 * NB - 1)

        @block.vector
        def _(dve):
            steps = [0]

            def then(ins):
                steps[0] += 1
                ins.then_inc(s_dve, 1)
                dve.wait_ge(s_dve, steps[0])

            def low(n, slot):
                for s in range(SLABS):
                    dve.wait_ge(s_hi, SLABS * n + (s + 1))
                    at = slice(TPS * s, TPS * s + TPS)
                    nc.vector.tensor_tensor(lo[:, slot, at], raw[:, slot, at], hi[:, slot, at],
                                            ALU.subtract).then_inc(s_lo, 1)

            def inverse(k):
                then(nc.vector.tensor_reduce(dtmp[:, 0], sums[:], AX_X, ALU.add))
                then(nc.vector.tensor_scalar(dtmp[:, 1], dtmp[:, 0], 0.0, None, ALU.is_gt))
                then(nc.vector.tensor_tensor(dtmp[:, 2], dtmp[:, 0], dtmp[:, 1], ALU.mult))
                then(nc.vector.tensor_scalar(dtmp[:, 1], dtmp[:, 1], -1.0, 1.0, ALU.mult, ALU.add))
                then(nc.vector.tensor_tensor(dtmp[:, 0], dtmp[:, 1], dtmp[:, 2], ALU.add))
                then(nc.vector.reciprocal(deg[:, k], dtmp[:, 0]))

            def scales():
                dve.wait_ge(s_small, 16 * len(small))
                then(nc.vector.tensor_tensor(ctmp[:], coef[:, 0], coef[:, 1], ALU.mult))
                then(nc.vector.tensor_tensor(ctmp[:], ctmp[:], coef[:, 0], ALU.mult))
                then(nc.vector.tensor_tensor(scale[:], ctmp[:, 0], ctmp[:, 1], ALU.add))
                for k in range(2, KD):
                    then(nc.vector.tensor_tensor(scale[:], scale[:], ctmp[:, k], ALU.add))

            def v_block(I):
                dve.wait_ge(s_w, I + 1)
                v = turned[:, I % 2].rearrange("p (t f) -> p t f", t=TPB)
                for t in range(TPB):
                    last = nc.vector.tensor_scalar(v[:, t], nat[:, I % 2, P * t:P * t + P],
                                                   scale[:, TPB * I + t:TPB * I + t + 1], None, ALU.mult)
                then(last)
                at = slice(TPB * I, TPB * I + TPB)
                then(nc.vector.tensor_copy(v_hi[:, at], v))
                nc.vector.tensor_tensor(v_lo[:, at], v, v_hi[:, at], ALU.subtract).then_inc(s_v, 1)
                for t in range(TPB * I, TPB * I + TPB):
                    last = nc.vector.tensor_tensor(rows[:, t], rows[:, t], bias_b[:], ALU.add)
                then(last)

            def o_sum(I):
                if I == NB - 1:
                    dve.wait_ge(s_rel, released(N1 - 1))
                    nc.vector.tensor_copy(turned[:, I % 2], accB[:, I % 2]).then_inc(s_os, 1)
                    return
                dve.wait_ge(s_o, NB - 1 - I)
                dve.wait_ge(s_os, I + 1)
                if NB - I - 2 > 0:
                    dve.wait_ge(s_t, NB - I - 2)
                nc.vector.tensor_tensor(turned[:, I % 2], accB[:, I % 2], part[:, I], ALU.add).then_inc(s_os, 1)

            def variance(I):
                for t in range(TPB):
                    last = nc.vector.bn_stats(stats[:, t], rows[:, TPB * I + t])
                then(last)
                for t in range(TPB):
                    last = nc.vector.bn_aggr(mv[:, t], stats[:, t])
                then(last)
                nc.vector.tensor_scalar(var[:], mv[:, :, 1], EPS, None, ALU.add).then_inc(s_var, 1)

            def normalize(I, k):
                dve.wait_ge(s_std, k + 1)
                then(nc.vector.reciprocal(rstd[:], std[:]))
                then(nc.vector.tensor_tensor(newt[:], var[:], rstd[:], ALU.mult))
                then(nc.vector.tensor_tensor(newt[:], newt[:], rstd[:], ALU.mult))
                then(nc.vector.tensor_scalar(newt[:], newt[:], -0.5, 1.5, ALU.mult, ALU.add))
                then(nc.vector.tensor_tensor(rstd[:], rstd[:], newt[:], ALU.mult))
                for t in range(TPB):
                    last = nc.vector.tensor_scalar(rows[:, TPB * I + t], rows[:, TPB * I + t], mv[:, t, 0:1],
                                                   rstd[:, t:t + 1], ALU.subtract, ALU.mult)
                return last

            def x1_block(I):
                at = slice(TPB * I, TPB * I + TPB)
                dve.wait_ge(s_t, NB - I)
                ins = nc.vector.tensor_tensor(rows[:, at], nat[:, I % 2].rearrange("p (t f) -> p t f", t=TPB),
                                              rows[:, at], ALU.add)
                ins.then_inc(s_nat, 1)
                dve.wait_ge(s_nat, NB - I)
                variance(I)

            def x1_parts(I):
                at = slice(TPB * I, TPB * I + TPB)
                then(normalize(I, NB - 1 - I))
                then(nc.vector.tensor_copy(x_hi[:, at], rows[:, at]))
                nc.vector.tensor_tensor(x_lo[:, at], rows[:, at], x_hi[:, at], ALU.subtract).then_inc(s_x1, 1)

            def h_block(J, b):
                dve.wait_ge(s_w, NB + 1 + J)
                for t in range(TPB):
                    row = rows[:, bass.ds(TPB * J + t, 1)]
                    last = nc.vector.scalar_tensor_tensor(row, nat[:, b, P * t:P * t + P],
                                                          deg[:, 0, bass.ds(TPB * J + t, 1)], row,
                                                          ALU.mult, ALU.add)
                last.then_inc(s_nat, 1)

            def out_block(I):
                dve.wait_ge(s_w, 2 * NB + I + 1)
                dve.wait_ge(s_nat, 2 * NB)
                for t in range(TPB):
                    r = TPB * I + t
                    last = nc.vector.scalar_tensor_tensor(rows[:, r], nat[:, I % 2, P * t:P * t + P],
                                                          deg[:, 1, r:r + 1], rows[:, r], ALU.mult, ALU.add)
                last.then_inc(s_nat, 1)
                dve.wait_ge(s_nat, 2 * NB + I + 1)
                variance(I)

            def beside(n):
                if n == NB + 1:
                    scales()
                if n in z_at:
                    v_block(z_at[n])
                if n - 3 in last1 and n - 3 < N1 - 1:
                    I = last1[n - 3]
                    dve.wait_ge(s_rel, released(n - 3))
                    nc.vector.tensor_copy(part[:, I], accB[:, I % 2]).then_inc(s_os, 1)
                if n == N1 + 1:
                    o_sum(NB - 1)
                if n in sum_at:
                    o_sum(sum_at[n])
                if n in norm_at:
                    x1_block(norm_at[n])
                if n in parts_at:
                    x1_parts(parts_at[n])
                if n == N1 + 5:
                    inverse(0)

            def block3(J, b, first=False):
                for k in range(NB):
                    n = N2 + NB * J + k
                    low(n, k % RING)
                    if first:
                        beside(n)
                    elif k == 2:
                        h_block(J - 1, 1 - b)

            for n in range(N2):
                if n < NB:
                    b = phase1[n][0]
                    at = slice(TPB * b, TPB * b + TPB)
                    dve.wait_ge(s_xhi, n + 1)
                    nc.vector.tensor_tensor(x_lo[:, at], rows[:, at], x_hi[:, at],
                                            ALU.subtract).then_inc(s_xlo, 1)
                low(n, n % RING)
                beside(n)
            block3(0, 0, first=True)
            block3(1, 1)
            with dve.Fori(1, NB // 2) as pair:
                block3(2 * pair, 0)
                block3(2 * pair + 1, 1)
            for n in range(N3, N4):
                low(n, n % RING)
                if n == N3:
                    inverse(1)
                if n == N3 + 2:
                    h_block(NB - 1, 1)
                if n - 5 in last4:
                    normalize(last4[n - 5], NB + last4[n - 5]).then_inc(s_out, 1)
                if n - 4 in last4:
                    out_block(last4[n - 4])
            out_block(NB - 1)
            normalize(NB - 1, 2 * NB - 1).then_inc(s_out, 1)

        @block.tensor
        def _(pe):
            def product(acc, r_hi, r_lo, K, n, first, last, slot=None):
                slot = n % RING if slot is None else slot
                for s in range(SLABS):
                    tiles = range(TPS * s, TPS * s + TPS)
                    pe.wait_ge(s_hi, SLABS * n + (s + 1))
                    for t in tiles:
                        nc.tensor.matmul(acc, r_hi[:, TPB * K + t], hi[:, slot, t],
                                         start=(first and t == 0), stop=False)
                        nc.tensor.matmul(acc, r_lo[:, TPB * K + t], hi[:, slot, t], start=False, stop=False)
                    pe.wait_ge(s_lo, SLABS * n + (s + 1))
                    for t in tiles:
                        mm = nc.tensor.matmul(acc, r_hi[:, TPB * K + t], lo[:, slot, t], start=False,
                                              stop=(last and t == TPB - 1))
                return mm

            def by_rows(b, w, more=None):
                for t in range(TPB):
                    to = slice(P * t, P * t + P)
                    if more is not None:
                        nc.tensor.matmul(nat[:, b, to], more[:, to], w[:], start=True, stop=False)
                    mm = nc.tensor.matmul(nat[:, b, to], turned[:, b, to], w[:], start=more is None, stop=True)
                mm.then_inc(s_w, 1)

            def w0_block(I):
                pe.wait_ge(s_zt, I + 1)
                pe.wait_ge(s_small, 16 * len(small))
                if I >= 2:
                    pe.wait_ge(s_v, I - 1)
                by_rows(I % 2, w0)

            def diagonal(I):
                pe.wait_ge(s_v, I + 1)
                product(accB[:, I % 2], v_hi, v_lo, I, NB * I + NB - 1, I == 0, True).then_inc(s_rel, 1)

            def transposes(I):
                pe.wait_ge(s_os, 2 * NB - 1 - I)
                if NB - I - 2 > 0:
                    pe.wait_ge(s_nat, NB - I - 2)
                for t in range(TPB):
                    mm = nc.tensor.transpose(nat[:, I % 2, P * t:P * t + P], turned[:, I % 2, P * t:P * t + P],
                                             ident[:])
                mm.then_inc(s_t, 1)

            def convolve2(n):
                J, I = chunks[n]
                pe.wait_ge(s_x1, NB - J)
                if J == NB - 1 and NB - 3 - I > 0:
                    pe.wait_ge(s_ys, NB - 3 - I)
                product(accA[:, I % 2], x_hi, x_lo, J, n, J == NB - 1, J == I + 1).then_inc(s_rel, 1)

            def propagate(n):
                J, I = chunks[n]
                pe.wait_ge(s_v, J + 1)
                if J == 0 and I >= 2:
                    pe.wait_ge(s_os, I - 1)
                product(accB[:, I % 2], v_hi, v_lo, J, n, J == 0, False).then_inc(s_rel, 1)

            for n in range(N1):
                J, I = chunks[n]
                if n < NB:
                    pe.wait_ge(s_xlo, n + 1)
                if n % NB == 0 and I >= 2:
                    pe.wait_ge(s_zt, I - 1)
                mm = product(accA[:, I % 2], x_hi, x_lo, J, n, n % NB == 0, J == I)
                if J == I:
                    mm.then_inc(s_z1, 1)
                elif J > I:
                    mm.then_inc(s_rel, 1)
                elif n < N1 - 1 - HELD:
                    propagate(n)
                if n >= NB and n % NB == 0:
                    w0_block(I - 1)
                if n >= NB and n % NB == 1:
                    diagonal(I - 1)
            propagate(N1 - 3)
            w0_block(NB - 1)
            propagate(N1 - 2)
            diagonal(NB - 1)

            for n in range(N1, N2):
                J, I = chunks[n]
                if J == NB - 1:
                    pe.wait_ge(s_os, 2 * NB - 3 - I)
                mm = product(accB[:, I % 2], v_hi, v_lo, J, n, J == NB - 1, J == I + 1)
                if J == I + 1:
                    mm.then_inc(s_o, 1)
                if n in turn_at:
                    transposes(turn_at[n])
                if n >= N1 + LAG:
                    convolve2(n - LAG)
            convolve2(N2 - 2)
            transposes(0)
            convolve2(N2 - 1)

            def w_out_block(J, b):
                pe.wait_ge(s_zt, NB + 1 + J)
                if isinstance(J, int) and J < 2:
                    pe.wait_ge(s_nat, NB)
                else:
                    pe.wait_ge(s_nat, NB - 1 + J)
                by_rows(b, w_out)

            def block3(J, b, first=False):
                for k in range(NB):
                    n = N2 + NB * J + k
                    I = NB - 1 - k
                    if first:
                        pe.wait_ge(s_x1, NB - I)
                    if k == 0 and not (isinstance(J, int) and J < 2):
                        pe.wait_ge(s_zt, NB - 1 + J)
                    product(accB[:, b], x_hi, x_lo, I, n, k == 0, I == 0, k % RING).then_inc(s_rel, 1)
                    if k == 1 and not first:
                        w_out_block(J - 1, 1 - b)

            def w_in_block(I):
                pe.wait_ge(s_y4s, I + 1)
                pe.wait_ge(s_nat, 2 * NB - 1 + I)
                by_rows(I % 2, w_in, part[:, I] if I < NB - 1 else None)

            block3(0, 0, first=True)
            block3(1, 1)
            with pe.Fori(1, NB // 2) as pair:
                block3(2 * pair, 0)
                block3(2 * pair + 1, 1)

            for n in range(N3, N4):
                J, I = chunks[n]
                if J == 0:
                    pe.wait_ge(s_ys, NB - 1)
                    if I >= 2:
                        pe.wait_ge(s_y4s, I - 1)
                product(accA[:, I % 2], x_hi, x_lo, J, n, J == 0, J == I).then_inc(s_rel, 1)
                if n == N3 + 1:
                    w_out_block(NB - 1, 1)
                if n - 2 in last4:
                    w_in_block(last4[n - 2])
            w_in_block(NB - 1)


def kernel(x, adj, L0_gnn_d_list, L0_gnn_weight, L0_gnn_filt, L0_gnn_bias, L1_gnn_W_in, L1_gnn_W_out):
    import numpy as np
    import concourse.bacc as bacc
    from concourse import mybir
    from concourse.bass_utils import run_bass_kernel_spmd

    x, adj = np.asarray(x), np.asarray(adj)
    N, F = x.shape
    NB, NT = N // BLK, N // P
    levels = [np.asarray(a).reshape(-1, NT, P).transpose(2, 0, 1) for a in (L0_gnn_d_list, L0_gnn_filt)]
    arrays = {
        "x_t": x.reshape(NT, P, F).transpose(1, 0, 2),
        "adj_b": adj.reshape(NB, TPB, P, NB, BLK).transpose(0, 3, 2, 1, 4),
        "adjT_b": adj.reshape(NB, BLK, NB, TPB, P).transpose(2, 0, 4, 3, 1),
        "coef_t": np.stack(levels, axis=1),
        "W0": np.asarray(L0_gnn_weight),
        "bias": np.asarray(L0_gnn_bias),
        "W_in": np.asarray(L1_gnn_W_in),
        "W_out": np.asarray(L1_gnn_W_out),
        "ident": np.eye(P, dtype=np.float32),
    }
    nc = bacc.Bacc("TRN2", target_bir_lowering=False, num_devices=1)
    named, args = {}, []
    for name, a in arrays.items():
        named[f"in_{name}"] = np.ascontiguousarray(a)
        args.append(nc.dram_tensor(f"in_{name}", a.shape, mybir.dt.from_np(a.dtype), kind="ExternalInput").ap())
    args.append(nc.dram_tensor("out", (N, F), mybir.dt.float32, kind="ExternalOutput").ap())
    graph_kernel(nc, *args)
    return run_bass_kernel_spmd(nc, [named], core_ids=[0]).results[0]["out"]
```
